# Optimizing a Trainium2 kernel written in Bass

```python
import numpy as np
import jax
import jax.numpy as jnp

def _softmax(x, axis=-1):
    return jax.nn.softmax(x, axis=axis)

def _gelu(x):
    return jax.nn.gelu(x, approximate=True)

def _silu(x):
    return jax.nn.silu(x)

def _sigmoid(x):
    return jax.nn.sigmoid(x)

def _layernorm(x, axis=-1, eps=1e-05):
    m = jnp.mean(x, axis=axis, keepdims=True)
    v = jnp.var(x, axis=axis, keepdims=True)
    return (x - m) / jnp.sqrt(v + eps)

def _scatter_add(tgt, idx, src, axis=0):
    return tgt.at[idx].add(src)

def _segment_sum(src, seg, n):
    return jax.ops.segment_sum(src, seg, n)
kernel_name = 'mk_seq_postln_d2_jaxref_r8_320b33'

def setup_inputs(seed: int=0):
    np.random.seed(seed)
    _w = jnp.asarray

    def _L0_attn_setup():
        import jax, jax.numpy as jnp
        import numpy as np
        D_MODEL, N_HEADS, N_KV, HEAD_DIM, D_LAT = (128, 8, 2, 128, 32)
        N_REP = N_HEADS // N_KV
        B, T = (2, 256)
        key = jax.random.key(seed)
        ks = jax.random.split(key, 8)
        s = lambda fan_in: 1.0 / np.sqrt(fan_in)
        return {'x': jax.random.normal(ks[0], (B, T, D_MODEL), jnp.float32), 'wq': jax.random.normal(ks[1], (D_MODEL, N_HEADS * HEAD_DIM), jnp.float32) * s(D_MODEL), 'wk_down': jax.random.normal(ks[2], (D_MODEL, N_KV * D_LAT), jnp.float32) * s(D_MODEL), 'wv_down': jax.random.normal(ks[3], (D_MODEL, N_KV * D_LAT), jnp.float32) * s(D_MODEL), 'wk_up': jax.random.normal(ks[4], (D_LAT, HEAD_DIM), jnp.float32) * s(D_LAT), 'wv_up': jax.random.normal(ks[5], (D_LAT, HEAD_DIM), jnp.float32) * s(D_LAT), 'wo': jax.random.normal(ks[6], (N_HEADS * HEAD_DIM, D_MODEL), jnp.float32) * s(N_HEADS * HEAD_DIM)}
    _L0_attn_in = _L0_attn_setup()

    def _L0_ffn_setup():
        import jax, jax.numpy as jnp
        import numpy as np
        BLOCK = 16
        _GRID = jnp.array([0.0, 0.5, 1.0, 1.5, 2.0, 3.0, 4.0, 6.0], dtype=jnp.float32)
        _MID = jnp.array([0.25, 0.75, 1.25, 1.75, 2.5, 3.5, 5.0], dtype=jnp.float32)

        def fp4_quant_dequant(x):
            shape = x.shape
            xb = x.reshape(shape[:-1] + (shape[-1] // BLOCK, BLOCK))
            scale = jnp.max(jnp.abs(xb), axis=-1, keepdims=True) / 6.0
            scale = jnp.maximum(scale, jnp.float32(1e-12))
            xn = xb / scale
            idx = jnp.searchsorted(_MID, jnp.abs(xn))
            q = _GRID[idx] * jnp.sign(xn) * scale
            return q.reshape(shape)

        def fp4_linear(x, w):
            xq = fp4_quant_dequant(x)
            wq = fp4_quant_dequant(w)
            return jnp.einsum('bsk,nk->bsn', xq, wq)
        key = jax.random.key(seed)
        k1, k2, k3, k4 = jax.random.split(key, 4)
        H, I = (128, 352)
        x = jax.random.normal(k1, (4, 512, H), dtype=jnp.float32)
        w_gate = jax.random.normal(k2, (I, H), dtype=jnp.float32) * 0.02
        w_up = jax.random.normal(k3, (I, H), dtype=jnp.float32) * 0.02
        w_down = jax.random.normal(k4, (H, I), dtype=jnp.float32) * 0.02
        return {'x': x, 'w_gate': w_gate, 'w_up': w_up, 'w_down': w_down}
    _L0_ffn_in = _L0_ffn_setup()

    def _L1_attn_setup():
        import jax, jax.numpy as jnp
        import numpy as np
        B, N, D = (2, 256, 128)
        H, G = (16, 4)
        HD = D // H
        key = jax.random.key(seed)
        ks = jax.random.split(key, 9)
        s = 0.02
        return {'x': jax.random.normal(ks[0], (B, N, D), dtype=jnp.float32), 'Wq': jax.random.normal(ks[1], (D, D), dtype=jnp.float32) * s, 'bq': jax.random.normal(ks[2], (D,), dtype=jnp.float32) * s, 'Wk': jax.random.normal(ks[3], (G * HD, D), dtype=jnp.float32) * s, 'bk': jax.random.normal(ks[4], (G * HD,), dtype=jnp.float32) * s, 'Wv': jax.random.normal(ks[5], (G * HD, D), dtype=jnp.float32) * s, 'bv': jax.random.normal(ks[6], (G * HD,), dtype=jnp.float32) * s, 'Wo': jax.random.normal(ks[7], (D, D), dtype=jnp.float32) * s, 'bo': jax.random.normal(ks[8], (D,), dtype=jnp.float32) * s}
    _L1_attn_in = _L1_attn_setup()

    def _L1_ffn_setup():
        import jax, jax.numpy as jnp
        import numpy as np
        THRESHOLD = 0.1
        key = jax.random.key(seed)
        k1, k2, k3 = jax.random.split(key, 3)
        B, S, D, E = (4, 512, 128, 8)
        inputs = jax.random.normal(k1, (B, S, D), dtype=jnp.float32)
        gate_w = jax.random.normal(k2, (D, E), dtype=jnp.float32) * 0.02
        gate_b = jnp.zeros((E,), dtype=jnp.float32)
        expert_w = jax.random.normal(k3, (E, D, D), dtype=jnp.float32) * 0.02
        expert_b = jnp.zeros((E, D), dtype=jnp.float32)
        return {'inputs': inputs, 'gate_w': gate_w, 'gate_b': gate_b, 'expert_w': expert_w, 'expert_b': expert_b}
    _L1_ffn_in = _L1_ffn_setup()
    _d = {'L0_attn_x': _L0_attn_in['x'], 'L0_attn_wq': _L0_attn_in['wq'], 'L0_attn_wk_down': _L0_attn_in['wk_down'], 'L0_attn_wv_down': _L0_attn_in['wv_down'], 'L0_attn_wk_up': _L0_attn_in['wk_up'], 'L0_attn_wv_up': _L0_attn_in['wv_up'], 'L0_attn_wo': _L0_attn_in['wo'], 'L0_ffn_w_gate': _L0_ffn_in['w_gate'], 'L0_ffn_w_up': _L0_ffn_in['w_up'], 'L0_ffn_w_down': _L0_ffn_in['w_down'], 'L1_attn_Wq': _L1_attn_in['Wq'], 'L1_attn_bq': _L1_attn_in['bq'], 'L1_attn_Wk': _L1_attn_in['Wk'], 'L1_attn_bk': _L1_attn_in['bk'], 'L1_attn_Wv': _L1_attn_in['Wv'], 'L1_attn_bv': _L1_attn_in['bv'], 'L1_attn_Wo': _L1_attn_in['Wo'], 'L1_attn_bo': _L1_attn_in['bo'], 'L1_ffn_gate_w': _L1_ffn_in['gate_w'], 'L1_ffn_gate_b': _L1_ffn_in['gate_b'], 'L1_ffn_expert_w': _L1_ffn_in['expert_w'], 'L1_ffn_expert_b': _L1_ffn_in['expert_b']}
    _x0 = _d['L0_attn_x']
    _d['L0_attn_x'] = jax.random.normal(jax.random.fold_in(jax.random.key(seed), 1), (1, 2048, 128), dtype=_x0.dtype)
    del _x0
    return _d

def reference(L0_attn_x, L0_attn_wq, L0_attn_wk_down, L0_attn_wv_down, L0_attn_wk_up, L0_attn_wv_up, L0_attn_wo, L0_ffn_w_gate, L0_ffn_w_up, L0_ffn_w_down, L1_attn_Wq, L1_attn_bq, L1_attn_Wk, L1_attn_bk, L1_attn_Wv, L1_attn_bv, L1_attn_Wo, L1_attn_bo, L1_ffn_gate_w, L1_ffn_gate_b, L1_ffn_expert_w, L1_ffn_expert_b):

    def _L0_attn_ref(x, wq, wk_down, wv_down, wk_up, wv_up, wo):
        import jax, jax.numpy as jnp
        import numpy as np
        D_MODEL, N_HEADS, N_KV, HEAD_DIM, D_LAT = (128, 8, 2, 128, 32)
        N_REP = N_HEADS // N_KV
        B, T = (2, 256)
        Bq, Tq, _ = x.shape
        scale = HEAD_DIM ** (-0.5)
        q = (x @ wq).reshape(Bq, Tq, N_KV, N_REP, HEAD_DIM)
        k_lat = (x @ wk_down).reshape(Bq, Tq, N_KV, D_LAT)
        v_lat = (x @ wv_down).reshape(Bq, Tq, N_KV, D_LAT)
        k = jnp.einsum('bkhl,ld->bkhd', k_lat, wk_up)
        v = jnp.einsum('bkhl,ld->bkhd', v_lat, wv_up)
        scores = jnp.einsum('bqhrd,bkhd->bhrqk', q, k) * scale
        causal = jnp.tril(jnp.ones((Tq, Tq), dtype=bool))
        scores = jnp.where(causal, scores, jnp.finfo(scores.dtype).min)
        probs = jax.nn.softmax(scores, axis=-1)
        y = jnp.einsum('bhrqk,bkhd->bqhrd', probs, v)
        y = y.reshape(Bq, Tq, N_HEADS * HEAD_DIM)
        return y @ wo

    def _L0_ffn_ref(x, w_gate, w_up, w_down):
        import jax, jax.numpy as jnp
        import numpy as np
        BLOCK = 16
        _GRID = jnp.array([0.0, 0.5, 1.0, 1.5, 2.0, 3.0, 4.0, 6.0], dtype=jnp.float32)
        _MID = jnp.array([0.25, 0.75, 1.25, 1.75, 2.5, 3.5, 5.0], dtype=jnp.float32)

        def fp4_quant_dequant(x):
            shape = x.shape
            xb = x.reshape(shape[:-1] + (shape[-1] // BLOCK, BLOCK))
            scale = jnp.max(jnp.abs(xb), axis=-1, keepdims=True) / 6.0
            scale = jnp.maximum(scale, jnp.float32(1e-12))
            xn = xb / scale
            idx = jnp.searchsorted(_MID, jnp.abs(xn))
            q = _GRID[idx] * jnp.sign(xn) * scale
            return q.reshape(shape)

        def fp4_linear(x, w):
            xq = fp4_quant_dequant(x)
            wq = fp4_quant_dequant(w)
            return jnp.einsum('bsk,nk->bsn', xq, wq)
        gate = fp4_linear(x, w_gate)
        y = fp4_linear(x, w_up)
        h = jax.nn.silu(gate) * y
        return fp4_linear(h, w_down)

    def _L1_attn_ref(x, Wq, bq, Wk, bk, Wv, bv, Wo, bo):
        import jax, jax.numpy as jnp
        import numpy as np
        B, N, D = (2, 256, 128)
        H, G = (16, 4)
        HD = D // H
        b, n, d = x.shape
        hpg = H // G
        q = (x @ Wq.T + bq).reshape(b, n, G, hpg, HD)
        k = (x @ Wk.T + bk).reshape(b, n, G, HD)
        v = (x @ Wv.T + bv).reshape(b, n, G, HD)
        scale = 1.0 / jnp.sqrt(jnp.float32(HD))
        scores = jnp.einsum('bqghd,bkgd->bghqk', q, k) * scale
        attn = jax.nn.softmax(scores, axis=-1)
        y = jnp.einsum('bghqk,bkgd->bqghd', attn, v).reshape(b, n, d)
        return y @ Wo.T + bo

    def _L1_ffn_ref(inputs, gate_w, gate_b, expert_w, expert_b):
        import jax, jax.numpy as jnp
        import numpy as np
        THRESHOLD = 0.1
        d = inputs.shape[-1]
        x = inputs.reshape(-1, d)
        gate_logits = jax.nn.softmax(x @ gate_w + gate_b, axis=-1)
        selected = (gate_logits >= THRESHOLD).astype(x.dtype)
        weights = gate_logits * selected
        wsum = jnp.sum(weights, axis=-1, keepdims=True)
        weights = weights / jnp.where(wsum == 0, jnp.ones_like(wsum), wsum)
        E = expert_w.shape[0]
        out = jnp.zeros((x.shape[0], expert_w.shape[-1]), dtype=x.dtype)
        for e in range(E):
            out = out + weights[:, e:e + 1] * (x @ expert_w[e] + expert_b[e])
        return out.reshape(*inputs.shape[:-1], out.shape[-1])
    x = L0_attn_x
    x = _layernorm(x + _L0_attn_ref(x, L0_attn_wq, L0_attn_wk_down, L0_attn_wv_down, L0_attn_wk_up, L0_attn_wv_up, L0_attn_wo), axis=-1)
    x = _layernorm(x + _L0_ffn_ref(x, L0_ffn_w_gate, L0_ffn_w_up, L0_ffn_w_down), axis=-1)
    x = _layernorm(x + _L1_attn_ref(x, L1_attn_Wq, L1_attn_bq, L1_attn_Wk, L1_attn_bk, L1_attn_Wv, L1_attn_bv, L1_attn_Wo, L1_attn_bo), axis=-1)
    x = _layernorm(x + _L1_ffn_ref(x, L1_ffn_gate_w, L1_ffn_gate_b, L1_ffn_expert_w, L1_ffn_expert_b), axis=-1)
    return x

_drawn_inputs = setup_inputs


def setup_inputs(seed=0):
    import zlib

    import numpy as np

    out = dict(_drawn_inputs(seed))
    spreads = {'L1_ffn_gate_b': (0.0, 0.344), 'L1_ffn_expert_b': (0.0, 0.1)}
    factors = {'L0_ffn_w_gate': 5.368,
     'L0_ffn_w_up': 5.131,
     'L0_ffn_w_down': 5.165,
     'L1_attn_Wq': 8.0,
     'L1_attn_bq': 8.0,
     'L1_attn_Wk': 8.0,
     'L1_attn_bk': 64.0,
     'L1_attn_Wv': 8.0,
     'L1_attn_bv': 8.0,
     'L1_attn_Wo': 8.0,
     'L1_attn_bo': 4.474}
    for name, (base, spread) in spreads.items():
        noise = np.random.default_rng([zlib.crc32(name.encode()), seed]).standard_normal(out[name].shape)
        drawn = base * np.exp(spread * noise) if base else spread * noise
        out[name] = jnp.asarray(drawn.astype(out[name].dtype))
    for name, factor in factors.items():
        out[name] = (out[name] * factor).astype(out[name].dtype)
    return out
```

```python
import numpy as np
import concourse.bass as bass
from concourse import mybir
from contextlib import ExitStack

P = 128
T = 2048
D = 128
NT = T // P
QC = 512
NC = T // QC
QT = QC // P
HG = 4
LAT = 32
SHIFT = 3 * LAT
KR = SHIFT + 1
G0, G1 = 2, 4
HD0, HD1 = 128, 8
FF = 352
FB = 16
NE = 8
EPS = 1e-5
NEG = -1e30
VW0, VW1 = 64, 32
SIGN = 0x80000000
MAGNITUDE = 0x7fffffff
NP_RING = 8
CONST_W = 4 * P + 12


def constants():
    c = np.zeros((P, CONST_W), np.float32)
    i = np.arange(P)
    c[:, 0:P] = np.eye(P)
    c[:, P:2 * P] = np.where(i[:, None] > i[None, :], NEG, 0.0)
    c[:, 2 * P:3 * P] = np.where(i[None, :] > i[:, None], NEG, 0.0)
    for h in range(HG):
        c[:, 3 * P + h] = (i < SHIFT) & ((i % LAT) // HD1 == h)
    c[:, 3 * P + 4:3 * P + 8] = -0.5
    return c


def build(nc, A):
    f32, f32r, bf16, u32 = mybir.dt.float32, mybir.dt.float32r, mybir.dt.bfloat16, mybir.dt.uint32
    ACT, ALU, AX = mybir.ActivationFunctionType, mybir.AluOpType, mybir.AxisListType.X
    ctx = ExitStack()
    with ctx:
        def sb(name, shape, dt=f32):
            return ctx.enter_context(nc.sbuf_tensor(name, shape, dt))

        def sem(name):
            return ctx.enter_context(nc.semaphore(name))

        const = sb("const", [P, CONST_W])
        ident, head_mask, minus_half = const[:, 0:P], const[:, 3 * P:3 * P + 4], const[:, 3 * P + 4:3 * P + 8]
        ident_b = sb("ident_b", [P, P], bf16)
        mask_kq = sb("mask_kq", [P, P], bf16)
        mask_qk = sb("mask_qk", [P, P], bf16)
        X = sb("X", [P, NT, D])
        XT = sb("XT", [P, T])
        KO0 = sb("KO0", [KR, G0, T], f32r)
        KO1 = sb("KO1", [KR, G1, T], f32r)
        QO = sb("QO", [KR, 2, HG, QC], f32r)
        QF = sb("QF", [SHIFT, QC])
        QB = sb("QB", [SHIFT, QC], f32r)
        V0 = sb("V0", [P, NT, G0, VW0])
        V1 = sb("V1", [P, NT, G1, VW1])
        MP = sb("MP", [P, HG, QT, NC])
        MS = sb("MS", [P, HG, QT, KR])
        PR = sb("PR", [P, NP_RING, QC])
        OS = sb("OS", [P, QC])
        OR = sb("OR", [P, QT, HG])
        ON = sb("ON", [P, QT, D])
        ONT = sb("ONT", [P, G0, QC])
        R = sb("R", [P, QT, D])
        ST = sb("ST", [P, QT, 6])
        MV = sb("MV", [P, QT, 2])
        VE = sb("VE", [P, QT])
        RS = sb("RS", [P, QT])
        wq = sb("wq", [P, 1024])
        wkd = sb("wkd", [P, G0 * LAT])
        wvd = sb("wvd", [P, G0 * LAT])
        wup = sb("wup", [LAT, 2, HD0])
        wo = sb("wo", [P, 8, D])
        wqT = sb("wqT", [P, 8, D])
        wupT = sb("wupT", [P, 2, LAT])
        WQ3 = sb("WQ3", [P, 8, SHIFT])
        WK3 = sb("WK3", [P, G0, SHIFT])
        WVO = sb("WVO", [P, G0, D])
        wg = sb("wg", [P, 3, D])
        wu = sb("wu", [P, 3, D])
        wd = sb("wd", [P, FF])
        WGT = sb("WGT", [P, FF])
        WUT = sb("WUT", [P, FF])
        WDT = sb("WDT", [P, 3, D])
        NQ = QT * FF
        qa = sb("qa", [P, NQ])
        qt_ = sb("qt_", [P, NQ])
        qs = sb("qs", [P, NQ // FB])
        qr = sb("qr", [P, NQ // FB])
        H = sb("H", [P, QT, FF])
        UP = sb("UP", [P, QT, FF])
        XQ = sb("XQ", [P, QT, D])
        XQT = sb("XQT", [P, QC])
        HQT = sb("HQT", [P, QT, 3, P])
        Wq1, Wo1 = sb("Wq1", [P, D]), sb("Wo1", [P, D])
        Wkv1 = sb("Wkv1", [2 * LAT, D])
        WQ1T, WO1T = sb("WQ1T", [P, D]), sb("WO1T", [P, D])
        WKV1T = sb("WKV1T", [P, 2 * LAT])
        WQ13 = sb("WQ13", [P, G1, SHIFT])
        WK13 = sb("WK13", [P, G1, SHIFT])
        bq3 = sb("bq3", [SHIFT, G1])
        bk3 = sb("bk3", [SHIFT, G1])
        bv_b = sb("bv_b", [P, LAT])
        bo_b = sb("bo_b", [P, D])
        gb_b = sb("gb_b", [P, NE])
        gw = sb("gw", [P, NE])
        ew = sb("ew", [P, NE, D])
        eb = sb("eb", [NE, D])
        X2T = XQT
        ACC, OUT, GWT = XQ, UP[:, :, 0:D], HQT[0:NE, :, 0, :]
        GL = sb("GL", [P, QT, NE])
        GP = sb("GP", [P, QT, NE])
        G2 = sb("G2", [P, QT, NE])
        GM = sb("GM", [P, QT, 1])
        GS = sb("GS", [P, QT, 1])
        GW = sb("GW", [P, QT, NE])

        sign_bit = sb("sign_bit", [P, 1], u32)

        ps_s = ctx.enter_context(nc.psum_tensor("ps_s", [P, 4, QC], f32))
        ps_d = ctx.enter_context(nc.psum_tensor("ps_d", [P, 2, QC], f32))
        ps_o = ctx.enter_context(nc.psum_tensor("ps_o", [P, 2, QC], f32))

        ld = {n: sem("loaded_" + n) for n in ("x", "attn0", "ffn0", "attn1", "moe", "const")}
        side_full = sem("side_full")
        side_free = [sem("side_free0"), sem("side_free1")]
        made = sem("made")
        chain = sem("chain")
        score_full = sem("score_full")
        exp_done = sem("exp_done")
        pv_done = sem("pv_done")
        out_free = sem("out_free")
        weights_ready = sem("weights_ready")
        q_base = sem("q_base")
        q_ready = sem("q_ready")
        var_ready = sem("var_ready")
        rstd_ready = sem("rstd_ready")
        act_in = sem("act_in")
        act_out = sem("act_out")
        tile_out = sem("tile_out")
        stored = sem("stored")
        consts_set = sem("consts_set")

        block = ctx.enter_context(nc.Block())

        def next_queries(layer, c, g, it):
            if layer == 0:
                return [("q0", h, g, c, it % 2) for h in range(HG)]
            return [("q1", g, c, it % 2)]

        def maxima(layer, c, g, it):
            top = c + 1 if layer == 0 else NC
            return [("max", layer, h, q, kc, c, g, it % 2) for h in range(HG) for q in range(QT)
                    for kc in range(top)]

        def shifts(layer, c, g, it):
            return [("shift", layer, h, c, it % 2) for h in range(HG)]

        def before(layer, c, g, it):
            return next_queries(layer, c, g, it) + maxima(layer, c, g, it) + shifts(layer, c, g, it)

        def after0(c, g):
            return [("out0", b, c, g) for b in range(2)] + [("on0", g)]

        def chunk0(c):
            items = [("y0", c), ("xq", c)]
            for q in range(QT):
                items += [("gate", q), ("up", q)]
            items += [("hqT", q) for q in range(QT)]
            return items + [("down", c), ("x2T", c)]

        def chunk1(c):
            items = [("on1", c), ("y1", c), ("x3T", c), ("logits", c), ("gwT", c), ("ebias", c)]
            return items + [("expert", q, e) for q in range(QT) for e in range(2)]

        prep = ([("xT", t) for t in range(NC)] + [("wqT", b) for b in range(2)] + [("wupT",), ("fold_q",)]
                + [("fold_o",)] + [("k0", g, c) for g in range(G0) for c in range(NC)]
                + [("v0", t) for t in range(NC)] + [("wgT",), ("wuT",), ("wdT",)])
        mid = ([("w1T",)] + [("k1", g, c) for g in range(G1) for c in range(NC)] + [("v1",)])

        iters0 = [(c, g) for c in range(NC) for g in range(G0)]
        SCALE = (HD0 ** -0.5, HD1 ** -0.5)
        KO = (KO0, KO1)
        VO = (V0, V1)
        VW = (VW0, VW1)
        VN = (LAT + 1, HD1 + 1)

        def key_tiles(layer, c):
            return (c + 1) * QT if layer == 0 else NT

        def first_query(layer, c, kt):
            return max(0, kt - c * QT) * P if layer == 0 else 0

        def plan1(c, last):
            steps = []
            for g in range(G1):
                side = [] if g == 0 else [("out1", g - 1, g % 2 ^ 1)]
                if g < G1 - 1:
                    side = next_queries(1, c, g + 1, g + 1) + side + maxima(1, c, g + 1, g + 1) + \
                        shifts(1, c, g + 1, g + 1)
                elif not last:
                    side = next_queries(1, c + 1, 0, 0) + side + maxima(1, c + 1, 0, 0) + shifts(1, c + 1, 0, 0)
                steps.append((g, side))
            return steps, [("out1", G1 - 1, (G1 - 1) % 2)] + chunk1(c)

        steps1, tail1 = plan1(0, False)
        SIDE1 = sum(len(s) for _, s in steps1) + len(tail1)
        UNITS1 = G1 * NT * HG
        assert SIDE1 % 2 == 0
        units0 = [key_tiles(0, c) * HG for c, g in iters0]
        UNITS0 = sum(units0)

        side0 = prep + before(0, 0, 0, 0)
        for i, (c, g) in enumerate(iters0):
            if i + 1 < len(iters0):
                side0 += before(0, *iters0[i + 1], i + 1)
            side0 += after0(c, g) + (chunk0(c) if g == G0 - 1 else [])
        start1 = mid + before(1, 0, 0, 0)
        N_SIDE0 = len(side0) + len(start1)
        PAD = N_SIDE0 % 2
        BASE1 = N_SIDE0 + PAD

        FENCED = {"wqT", "fold_q", "fold_o", "k0", "k1", "on0", "on1", "y0", "y1", "gate", "down", "logits",
                  "ebias", "expert", "v1"}

        def fenced(item):
            return (item[0] in FENCED and item[0] not in ("gate", "expert")
                    or item[0] in ("gate", "expert") and item[1] == 0
                    or item[0] == "max" and item[1:5] == (0, 0, 0, 0))

        def is_made(item):
            return item[0] in ("shift", "out0", "out1", "xq", "x2T", "x3T", "gwT") or item[0] == "hqT" and item[1] == 0

        MADE1 = sum(is_made(i) for _, side in steps1 for i in side) + sum(is_made(i) for i in tail1)
        MADE0 = sum(is_made(i) for i in side0 + start1)

        @block.sync
        def _(sp):
            sp.dma_start(const[:, :], A["consts"]).then_inc(ld["const"], 16)
            sp.dma_start(X[:, :, :], A["L0_attn_x"].rearrange("b (t p) d -> p (b t) d", p=P)).then_inc(ld["x"], 16)
            for dst, src in ((wq[:, :], A["L0_attn_wq"]), (wkd[:, :], A["L0_attn_wk_down"]),
                             (wvd[:, :], A["L0_attn_wv_down"]), (wup[:, 0, :], A["L0_attn_wk_up"]),
                             (wup[:, 1, :], A["L0_attn_wv_up"]),
                             (wo[:, :, :], A["L0_attn_wo"].rearrange("(h p) d -> p h d", p=P))):
                sp.dma_start(dst, src).then_inc(ld["attn0"], 16)
            for dst, src in ((wg, A["L0_ffn_w_gate"]), (wu, A["L0_ffn_w_up"])):
                sp.dma_start(dst[:, 0:2, :], src[0:2 * P, :].rearrange("(t p) d -> p t d", p=P)).then_inc(ld["ffn0"], 16)
                sp.dma_start(dst[0:FF - 2 * P, 2, :], src[2 * P:FF, :]).then_inc(ld["ffn0"], 16)
            sp.dma_start(wd[:, :], A["L0_ffn_w_down"]).then_inc(ld["ffn0"], 16)
            sp.dma_start(Wq1[:, :], A["L1_attn_Wq"]).then_inc(ld["attn1"], 16)
            sp.dma_start(Wo1[:, :], A["L1_attn_Wo"]).then_inc(ld["attn1"], 16)
            sp.dma_start(Wkv1[0:LAT, :], A["L1_attn_Wk"]).then_inc(ld["attn1"], 16)
            sp.dma_start(Wkv1[LAT:2 * LAT, :], A["L1_attn_Wv"]).then_inc(ld["attn1"], 16)
            for r in range(3):
                sp.dma_start(bq3[r * LAT:(r + 1) * LAT, :],
                             A["L1_attn_bq"].rearrange("(g r) -> r g", g=G1), allow_slow_non_contiguous=True).then_inc(ld["attn1"], 16)
                for j in range(HG):
                    sp.dma_start(bk3[r * LAT + j * HD1:r * LAT + (j + 1) * HD1, :],
                                 A["L1_attn_bk"].rearrange("(g r) -> r g", g=G1), allow_slow_non_contiguous=True).then_inc(ld["attn1"], 16)
            for dst, name, n in ((bv_b, "L1_attn_bv", LAT), (bo_b, "L1_attn_bo", D)):
                sp.dma_start(dst[:, :], A[name].rearrange("(a n) -> a n", a=1).broadcast_to([P, n])).then_inc(ld["attn1"], 16)
            sp.dma_start(gb_b[:, :], A["L1_ffn_gate_b"].rearrange("(a n) -> a n", a=1).broadcast_to([P, NE])).then_inc(ld["moe"], 16)
            sp.dma_start(gw[:, :], A["L1_ffn_gate_w"]).then_inc(ld["moe"], 16)
            sp.dma_start(ew[:, :, :], A["L1_ffn_expert_w"].rearrange("e k n -> k e n")).then_inc(ld["moe"], 16)
            sp.dma_start(eb[:, :], A["L1_ffn_expert_b"]).then_inc(ld["moe"], 16)

            out_v = A["out"].rearrange("b (t p) d -> p (b t) d", p=P)

            def store(c):
                sp.wait_ge(tile_out, c + 1)
                sp.dma_start(out_v[:, bass.ds(c * QT, QT), :], OUT).then_inc(stored, 16)

            with sp.Fori(0, NC - 1) as c:
                store(c)
            store(NC - 1)
            sp.wait_ge(stored, 16 * (NC + 1))

        N_ATTN1 = 16 * (4 + 3 * (1 + HG) + 2)

        @block.tensor
        def _(pe):
            state = {"side": 0, "half": 0, "made": 0, "made_base": 0, "unit": 0, "ubase": 0}

            def bank_free(k):
                if k >= 0 or not isinstance(state["half"], int):
                    pe.wait_ge(side_free[k % 2], state["half"] + k // 2 + 1)

            def side_item(item):
                kind = item[0]
                k = state["side"]
                state["side"] = k + 1
                bank_free(k)
                if fenced(item):
                    bank_free(k + 1)
                if is_made(item):
                    state["made"] += 1
                    pe.wait_ge(made, state["made_base"] + state["made"])
                if kind == "max" and item[1] == 1 and item[2:5] == (0, 0, 0):
                    state["group"] = state["group"] + 1
                    pe.wait_ge(q_ready, state["group"])
                bank = ps_d[:, k % 2, :]
                last = None
                if kind == "xT":
                    t = item[1]
                    for j in range(QT):
                        last = nc.tensor.transpose(bank[:, j * P:(j + 1) * P], X[:, t * QT + j, :], ident)
                elif kind == "wqT":
                    for j in range(4):
                        h = item[1] * 4 + j
                        last = nc.tensor.transpose(bank[:, j * P:(j + 1) * P], wq[:, h * P:(h + 1) * P], ident)
                elif kind == "wupT":
                    for j in range(2):
                        last = nc.tensor.transpose(bank[:, j * LAT:(j + 1) * LAT], wup[:, j, :], ident[0:LAT, 0:LAT])
                elif kind == "fold_q":
                    for h in range(8):
                        last = nc.tensor.matmul(bank[:, h * LAT:(h + 1) * LAT], wqT[:, h, :], wupT[:, 0, :],
                                                start=True, stop=True)
                elif kind == "fold_o":
                    for h in range(8):
                        r = (h % HG) * LAT
                        last = nc.tensor.matmul(bank[r:r + LAT, (h // HG) * D:(h // HG + 1) * D], wupT[:, 1, :],
                                                wo[:, h, :], start=True, stop=True)
                elif kind in ("k0", "k1"):
                    g, c = item[1:]
                    w = WK3 if kind == "k0" else WK13
                    last = nc.tensor.matmul(bank[0:SHIFT, :], w[:, g, :], XT[:, c * QC:(c + 1) * QC],
                                            start=True, stop=True)
                elif kind == "v0":
                    for j in range(QT):
                        t = item[1] * QT + j
                        last = nc.tensor.matmul(bank[:, j * 64:(j + 1) * 64], XT[:, t * P:(t + 1) * P], wvd[:, :],
                                                start=True, stop=True)
                elif kind == "v1":
                    for t in range(NT):
                        last = nc.tensor.matmul(bank[:, t * LAT:(t + 1) * LAT], XT[:, t * P:(t + 1) * P],
                                                WKV1T[:, LAT:2 * LAT], start=True, stop=True)
                elif kind in ("wgT", "wuT"):
                    w = wg if kind == "wgT" else wu
                    for j in range(3):
                        n = min(P, FF - j * P)
                        last = nc.tensor.transpose(bank[:, j * P:j * P + n], w[0:n, j, :], ident[0:n, 0:n])
                elif kind == "wdT":
                    for j in range(3):
                        n = min(P, FF - j * P)
                        last = nc.tensor.transpose(bank[0:n, j * P:(j + 1) * P], wd[:, j * P:j * P + n], ident)
                elif kind == "w1T":
                    nc.tensor.transpose(bank[:, 0:P], Wq1[:, :], ident)
                    nc.tensor.transpose(bank[:, P:2 * P], Wo1[:, :], ident)
                    last = nc.tensor.transpose(bank[:, 2 * P:2 * P + 2 * LAT], Wkv1[:, :], ident[0:2 * LAT, 0:2 * LAT])
                elif kind == "q0":
                    h, g, c, _ = item[1:]
                    last = nc.tensor.matmul(bank[0:SHIFT, :], WQ3[:, g * HG + h, :], XT[:, c * QC:(c + 1) * QC],
                                            start=True, stop=True)
                elif kind == "q1":
                    g, c, _ = item[1:]
                    src = XT[:, c * QC:(c + 1) * QC] if isinstance(c, int) else XT[:, bass.ds(c * QC, QC)]
                    last = nc.tensor.matmul(bank[0:SHIFT, :], WQ13[:, g, :], src, start=True, stop=True)
                elif kind == "max":
                    layer, h, q, kc, c, g, par = item[1:]
                    n = (q + 1) * P if layer == 0 and kc == c else QC
                    causal = layer == 0 and kc == c
                    last = nc.tensor.matmul(bank[:, 0:n], QO[0:SHIFT, par, h, q * P:(q + 1) * P],
                                            KO[layer][0:SHIFT, g, kc * QC:kc * QC + n], start=True, stop=not causal)
                    if causal:
                        last = nc.tensor.matmul(bank[:, n - P:n], ident_b[:, :], mask_qk[:, :], start=False, stop=True)
                elif kind == "shift":
                    h = item[2]
                    for q in range(QT):
                        last = nc.tensor.transpose(bank[0:KR, q * P:(q + 1) * P], MS[:, h, q, :], ident)
                elif kind in ("out0", "out1"):
                    for q in range(QT):
                        last = nc.tensor.transpose(bank[:, q * P:(q + 1) * P], OS[:, q * P:(q + 1) * P], ident)
                elif kind == "on0":
                    for q in range(QT):
                        last = nc.tensor.transpose(bank[:, q * P:(q + 1) * P], ON[:, q, :], ident)
                elif kind == "on1":
                    for q in range(QT):
                        last = nc.tensor.transpose(bank[:, q * P:(q + 1) * P], ON[:, q, :], ident)
                elif kind == "y0":
                    for q in range(QT):
                        for g in range(G0):
                            last = nc.tensor.matmul(bank[:, q * D:(q + 1) * D], ONT[:, g, q * P:(q + 1) * P],
                                                    WVO[:, g, :], start=g == 0, stop=g == G0 - 1)
                elif kind == "y1":
                    for q in range(QT):
                        last = nc.tensor.matmul(bank[:, q * D:(q + 1) * D], ONT[:, 0, q * P:(q + 1) * P], WO1T[:, :],
                                                start=True, stop=True)
                elif kind == "xq":
                    for q in range(QT):
                        last = nc.tensor.transpose(bank[:, q * P:(q + 1) * P], XQ[:, q, :], ident)
                elif kind in ("gate", "up"):
                    q = item[1]
                    last = nc.tensor.matmul(bank[:, 0:FF], XQT[:, q * P:(q + 1) * P],
                                            (WGT if kind == "gate" else WUT)[:, :], start=True, stop=True)
                elif kind == "hqT":
                    q = item[1]
                    for j in range(3):
                        n = min(P, FF - j * P)
                        last = nc.tensor.transpose(bank[0:n, j * P:(j + 1) * P], H[:, q, j * P:j * P + n], ident)
                elif kind == "down":
                    for q in range(QT):
                        for j in range(3):
                            n = min(P, FF - j * P)
                            last = nc.tensor.matmul(bank[:, q * D:(q + 1) * D], HQT[0:n, q, j, :], WDT[0:n, j, :],
                                                    start=j == 0, stop=j == 2)
                elif kind == "x2T":
                    c = item[1]
                    for q in range(QT):
                        last = nc.tensor.transpose(bank[:, q * P:(q + 1) * P], X[:, c * QT + q, :], ident)
                elif kind == "x3T":
                    for q in range(QT):
                        last = nc.tensor.transpose(bank[:, q * P:(q + 1) * P], R[:, q, :], ident)
                elif kind == "logits":
                    for q in range(QT):
                        last = nc.tensor.matmul(bank[:, q * NE:(q + 1) * NE], X2T[:, q * P:(q + 1) * P], gw[:, :],
                                                start=True, stop=True)
                elif kind == "gwT":
                    for q in range(QT):
                        last = nc.tensor.transpose(bank[0:NE, q * P:(q + 1) * P], GW[:, q, :], ident)
                elif kind == "ebias":
                    for q in range(QT):
                        last = nc.tensor.matmul(bank[:, q * D:(q + 1) * D], GWT[:, q, :], eb[:, :],
                                                start=True, stop=True)
                elif kind == "expert":
                    q, e = item[1:]
                    last = nc.tensor.matmul(bank[:, :], X2T[:, q * P:(q + 1) * P], ew[:, 4 * e:4 * e + 4, :],
                                            start=True, stop=True)
                elif kind == "pad":
                    last = nc.tensor.matmul(bank[:, 0:P], ident_b[:, :], ident_b[:, :], start=True, stop=True)
                last.then_inc(side_full, 1)

            def iteration(layer, c, g, it, side):
                nk = key_tiles(layer, c)
                bank_free(state["side"])
                bank_free(state["side"] + 1)
                if layer == 1:
                    pe.wait_ge(out_free, 2 * len(iters0) + c * G1 + max(0, g - 1))
                elif it:
                    pe.wait_ge(out_free, 2 * it)
                u0 = state["unit"]

                def products(kt):
                    q0 = first_query(layer, c, kt)
                    for h in range(HG):
                        n = u0 + kt * HG + h
                        pe.wait_ge(exp_done, state["ubase"] + n + 5)
                        if layer == 0:
                            dst = ps_o[(h % 2) * VW0:(h % 2 + 1) * VW0, h // 2, q0:QC]
                        else:
                            dst = ps_o[h * VW1:(h + 1) * VW1, it % 2, q0:QC]
                        nc.tensor.matmul(dst, VO[layer][:, kt, g, :], PR[:, n % NP_RING, q0:QC],
                                         start=kt == 0, stop=kt == nk - 1).then_inc(pv_done, 1)

                for kt in range(nk):
                    q0 = first_query(layer, c, kt)
                    causal = layer == 0 and kt >= c * QT
                    for h in range(HG):
                        n = u0 + kt * HG + h
                        pe.wait_ge(exp_done, state["ubase"] + n + 1)
                        m = nc.tensor.matmul(ps_s[:, n % 4, q0:QC], KO[layer][:, g, kt * P:(kt + 1) * P],
                                             QO[:, it % 2, h, q0:QC], start=True, stop=not causal)
                        if causal:
                            m = nc.tensor.matmul(ps_s[:, n % 4, q0:q0 + P], ident_b[:, :], mask_kq[:, :],
                                                 start=False, stop=True)
                        m.then_inc(score_full, 1)
                    for item in side[len(side) * kt // nk:len(side) * (kt + 1) // nk]:
                        side_item(item)
                    if kt:
                        products(kt - 1)
                products(nk - 1)
                state["unit"] = u0 + nk * HG

            state["group"] = 0
            pe.wait_ge(ld["const"], 16)
            pe.wait_ge(ld["x"], 16)
            pe.wait_ge(ld["attn0"], 16 * 6)
            pe.wait_ge(ld["ffn0"], 16 * 5)
            pe.wait_ge(consts_set, 1)
            pe.wait_ge(weights_ready, 1)
            for item in prep + before(0, 0, 0, 0):
                side_item(item)
            for i, (c, g) in enumerate(iters0):
                nxt = before(0, *iters0[i + 1], i + 1) if i + 1 < len(iters0) else []
                iteration(0, c, g, i, nxt)
                for item in after0(c, g) + (chunk0(c) if g == G0 - 1 else []):
                    side_item(item)
            pe.wait_ge(ld["attn1"], N_ATTN1)
            pe.wait_ge(ld["moe"], 64)
            for item in start1 + [("pad",)] * PAD:
                side_item(item)

            assert state["side"] == BASE1

            def chunk(c, last):
                state.update(side=0, half=BASE1 // 2 + c * (SIDE1 // 2), made=0, made_base=MADE0 + c * MADE1,
                             unit=0, ubase=UNITS0 + c * UNITS1, group=c * G1 + 1)
                steps, tail = plan1(c, last)
                for g, side in steps:
                    iteration(1, c, g, g, side)
                for item in tail:
                    side_item(item)

            with pe.Fori(0, NC - 1) as c:
                chunk(c, False)
            chunk(NC - 1, True)

        @block.scalar
        def _(act):
            act.wait_ge(consts_set, 1)
            st = {"unit": 0, "ubase": 0}

            def exps(layer, c):
                for kt in range(key_tiles(layer, c)):
                    q0 = first_query(layer, c, kt)
                    for h in range(HG):
                        n = st["unit"]
                        act.wait_ge(score_full, st["ubase"] + n + 1)
                        act.wait_ge(pv_done, st["ubase"] + n + 1)
                        nc.scalar.activation(PR[:, n % NP_RING, q0:QC], ps_s[:, n % 4, q0:QC], ACT.Exp,
                                             scale=SCALE[layer]).then_inc(exp_done, 1)
                        st["unit"] = n + 1

            for c, g in iters0:
                exps(0, c)
                if g == G0 - 1:
                    act.wait_ge(act_in, c + 1)
                    nc.scalar.activation(H[:, :, :], H[:, :, :], ACT.Silu).then_inc(act_out, 1)

            def chunk(c):
                st.update(unit=0, ubase=UNITS0 + c * UNITS1)
                for g in range(G1):
                    exps(1, c)
                act.wait_ge(act_in, NC + c + 1)
                nc.scalar.activation(GP[:, :, :], GL[:, :, :], ACT.Exp).then_inc(act_out, 1)

            with act.Fori(0, NC - 1) as c:
                chunk(c)
            chunk(NC - 1)

        @block.gpsimd
        def _(pool):
            nc.gpsimd.memset(V0[:, :, :, :], 1.0).then_inc(stored, 16)
            nc.gpsimd.memset(V1[:, :, :, :], 1.0).then_inc(exp_done, 4)
            nc.gpsimd.memset(MS[:, :, :, :], 0.0).then_inc(pv_done, NP_RING)
            nc.gpsimd.memset(RS[:, :], 0.0).then_inc(side_free[0], 1)
            nc.gpsimd.memset(VE[:, :], 0.0).then_inc(side_free[1], 1)
            pool.wait_ge(side_free[1], 1)
            nc.gpsimd.memset(sign_bit[:, :], SIGN).then_inc(consts_set, 1)

            def rstd(n):
                pool.wait_ge(var_ready, n)
                nc.gpsimd.tensor_tensor(RS[:, :], VE[:, :], minus_half, ALU.pow).then_inc(rstd_ready, 1)

            def masked(n, par):
                pool.wait_ge(q_base, n)
                nc.gpsimd.tensor_tensor(QO[0:SHIFT, par, 0, :], QB[:, :].bitcast(f32),
                                        head_mask[0:SHIFT, 0:1].broadcast_to([SHIFT, QC]), ALU.mult)
                for h in range(1, HG):
                    m = nc.gpsimd.tensor_scalar(QO[0:SHIFT, par, h, :], QB[:, :].bitcast(f32), head_mask[0:SHIFT, h:h + 1],
                                                1.0, ALU.mult, ALU.mult)
                m.then_inc(q_ready, 1)

            pool.wait_ge(ld["const"], 16)
            for c in range(NC):
                rstd(2 * c + 1)
                rstd(2 * c + 2)
            masked(1, 0)

            def chunk(c, last):
                for g in range(G1):
                    if not (last and g == G1 - 1):
                        masked(c * G1 + g + 2, (g + 1) % 2)
                rstd(2 * NC + 2 * c + 1)
                rstd(2 * NC + 2 * c + 2)

            with pool.Fori(0, NC - 1) as c:
                chunk(c, False)
            chunk(NC - 1, True)

        @block.vector
        def _(dve):
            v = nc.vector
            S = {"side": 0, "base": 0, "half": 0, "links": 0, "rstd": 0, "act": 0, "group": None,
                 "units": NP_RING}

            def link(ins):
                S["links"] += 1
                ins.then_inc(chain, 1)
                dve.wait_ge(chain, S["links"])

            def full():
                k = S["side"]
                S["side"] = k + 1
                dve.wait_ge(side_full, S["base"] + k + 1)
                return ps_d[:, k % 2, :], side_free[k % 2]

            def settled():
                k = S["side"] - 1
                if k >= 0 or not isinstance(S["half"], int):
                    dve.wait_ge(side_free[k % 2], S["half"] + k // 2 + 2)

            def quantise(out, src, rows, width, sgn=None):
                nb = width // FB
                s, a, t = src, qa[0:rows, 0:width], qt_[0:rows, 0:width]
                sc, rc = qs[0:rows, 0:nb], qr[0:rows, 0:nb]
                blk = lambda x: x.rearrange("p (n b) -> p n b", b=FB)
                bc = lambda x: x.unsqueeze(2).broadcast_to([rows, nb, FB])
                link(v.tensor_reduce(sc, blk(s), AX, ALU.max, apply_absolute_value=True))
                link(v.tensor_scalar(sc, sc, 1.0 / 6.0, 1e-12, ALU.mult, ALU.max))
                link(v.reciprocal(rc, sc))
                link(v.tensor_tensor(blk(a), blk(s), bc(rc), ALU.mult))
                link(v.tensor_scalar(a.bitcast(u32), a.bitcast(u32), MAGNITUDE, None, ALU.bitwise_and))
                link(v.tensor_scalar(t, a, 5.0, 2.0, ALU.is_gt, ALU.mult))
                link(v.scalar_tensor_tensor(t, a, 3.5, t, ALU.is_gt, ALU.add))
                link(v.scalar_tensor_tensor(t, a, 2.5, t, ALU.is_gt, ALU.add))
                link(v.tensor_scalar(t, t, 2.0, None, ALU.mult))
                for mid_ in (1.75, 1.25, 0.75, 0.25):
                    link(v.scalar_tensor_tensor(t, a, mid_, t, ALU.is_gt, ALU.add))
                link(v.scalar_tensor_tensor(blk(a), blk(t), 0.5, bc(sc), ALU.mult, ALU.mult))
                link(v.scalar_tensor_tensor(out.bitcast(u32), s.bitcast(u32), sign_bit[0:rows, :], a.bitcast(u32),
                                            ALU.bitwise_and, ALU.bitwise_or))

            def layernorm(out):
                for q in range(QT):
                    i = v.bn_stats(ST[:, q, :], R[:, q, :])
                link(i)
                for q in range(QT):
                    i = v.bn_aggr(MV[:, q, :], ST[:, q, :])
                link(i)
                v.tensor_scalar(VE[:, :], MV[:, :, 1], EPS, None, ALU.add).then_inc(var_ready, 1)
                S["rstd"] = S["rstd"] + 1
                dve.wait_ge(rstd_ready, S["rstd"])
                for q in range(QT):
                    i = v.tensor_scalar(out[:, q, :], R[:, q, :], MV[:, q, 0:1], RS[:, q:q + 1], ALU.subtract, ALU.mult)
                link(i)


            def unsplit(bank, bias=None):
                if bias is None:
                    link(v.tensor_copy(QF[:, :], bank[0:SHIFT, :]))
                else:
                    link(v.tensor_scalar(QF[:, :], bank[0:SHIFT, :], bias, None, ALU.add))

            def heads_and_tails(dst, tail):
                link(v.tensor_copy(dst, QF[:, :]))
                lo = slice(tail * LAT, (tail + 1) * LAT)
                return v.tensor_tensor(dst[lo, :], QF[lo, :], dst[lo, :].bitcast(f32), ALU.subtract)

            def side_item(item):
                kind = item[0]
                if kind != "max" or item[2:5] == (0, 0, 0):
                    settled()
                if is_made(item):
                    make(item)
                bank, free = full()
                if kind == "xT":
                    v.tensor_copy(XT[:, item[1] * QC:(item[1] + 1) * QC], bank).then_inc(free, 1)
                elif kind == "wqT":
                    v.tensor_copy(wqT[:, 4 * item[1]:4 * item[1] + 4, :], bank.rearrange("p (h d) -> p h d", d=D)).then_inc(free, 1)
                elif kind == "wupT":
                    v.tensor_copy(wupT[:, :, :], bank[:, 0:2 * LAT].rearrange("p (h d) -> p h d", d=LAT)).then_inc(free, 1)
                elif kind == "fold_q":
                    for r in range(3):
                        i = v.tensor_copy(WQ3[:, :, r * LAT:(r + 1) * LAT], bank[:, 0:8 * LAT].rearrange("p (h d) -> p h d", d=LAT))
                    i.then_inc(free, 1)
                elif kind == "fold_o":
                    v.tensor_copy(WVO[:, :, :], bank[:, 0:G0 * D].rearrange("p (g d) -> p g d", d=D)).then_inc(free, 1)
                elif kind in ("k0", "k1"):
                    g, c = item[1:]
                    unsplit(bank, None if kind == "k0" else bk3[:, g:g + 1])
                    heads_and_tails(KO[kind == "k1"][0:SHIFT, g, c * QC:(c + 1) * QC], 1).then_inc(free, 1)
                elif kind == "v0":
                    t = item[1]
                    for g in range(G0):
                        i = v.tensor_copy(V0[:, t * QT:(t + 1) * QT, g, 0:LAT],
                                          bank[:, 0:QT * 64].rearrange("p (t g l) -> p t g l", t=QT, g=G0)[:, :, g, :])
                    i.then_inc(free, 1)
                elif kind == "v1":
                    for g in range(G1):
                        i = v.tensor_tensor(V1[:, :, g, 0:HD1],
                                            bank.rearrange("p (t g l) -> p t g l", t=NT, g=G1)[:, :, g, :],
                                            bv_b[:, g * HD1:(g + 1) * HD1].unsqueeze(1).broadcast_to([P, NT, HD1]), ALU.add)
                    i.then_inc(free, 1)
                elif kind in ("wgT", "wuT"):
                    v.tensor_copy((WGT if kind == "wgT" else WUT)[:, :], bank[:, 0:FF]).then_inc(free, 1)
                elif kind == "wdT":
                    v.tensor_copy(WDT[:, 0:2, :], bank[:, 0:2 * P].rearrange("p (j d) -> p j d", d=D))
                    v.tensor_copy(WDT[0:FF - 2 * P, 2, :], bank[0:FF - 2 * P, 2 * P:3 * P]).then_inc(free, 1)
                elif kind == "w1T":
                    v.tensor_copy(WQ1T[:, :], bank[:, 0:P])
                    v.tensor_copy(WO1T[:, :], bank[:, P:2 * P])
                    link(v.tensor_copy(WKV1T[:, :], bank[:, 2 * P:2 * P + 2 * LAT]))
                    for g in range(G1):
                        for r in range(3):
                            v.tensor_copy(WQ13[:, g, r * LAT:(r + 1) * LAT], WQ1T[:, g * LAT:(g + 1) * LAT])
                        i = v.tensor_copy(WK13[:, g, :].rearrange("p (r l) -> p r l", l=HD1),
                                          WKV1T[:, g * HD1:(g + 1) * HD1].unsqueeze(1).broadcast_to([P, 3 * HG, HD1]))
                    i.then_inc(free, 1)
                elif kind == "q0":
                    h, g, c, par = item[1:]
                    unsplit(bank)
                    heads_and_tails(QO[0:SHIFT, par, h, :], 2).then_inc(free, 1)
                elif kind == "q1":
                    g, c, par = item[1:]
                    unsplit(bank, bq3[:, g:g + 1])
                    if S["group"] is not None:
                        dve.wait_ge(q_ready, S["group"])
                    S["group"] = 1 if S["group"] is None else S["group"] + 1
                    link(v.tensor_copy(QB[:, :], QF[:, :]))
                    link(v.tensor_tensor(QB[2 * LAT:SHIFT, :], QF[2 * LAT:SHIFT, :], QB[2 * LAT:SHIFT, :].bitcast(f32),
                                         ALU.subtract))
                    v.engine_nop().then_inc(q_base, 1)
                    v.engine_nop().then_inc(free, 1)
                elif kind == "max":
                    layer, h, q, kc, c, g, par = item[1:]
                    n = (q + 1) * P if layer == 0 and kc == c else QC
                    v.tensor_reduce(MP[:, h, q, kc:kc + 1], bank[:, 0:n], AX, ALU.max).then_inc(free, 1)
                elif kind == "shift":
                    layer, h, c, par = item[1:]
                    v.tensor_copy(QO[SHIFT:KR, par, h, :], bank[SHIFT:KR, :]).then_inc(free, 1)
                else:
                    chunk_item(item, bank, free)

            def make(item):
                kind = item[0]
                if kind == "shift":
                    layer, h, c, par = item[1:]
                    top = c + 1 if layer == 0 else NC
                    v.tensor_reduce(MS[:, h, :, SHIFT], MP[:, h, :, 0:top], AX, ALU.max, negate=True).then_inc(made, 1)
                elif kind in ("out0", "out1"):
                    if kind == "out0":
                        b = item[1]
                    else:
                        b = item[2]
                    dve.wait_ge(pv_done, S["pv"])
                    link(v.tensor_copy(OS[:, :], ps_o[:, b, :]))
                    v.engine_nop().then_inc(out_free, 1)
                    v.engine_nop().then_inc(made, 1)
                elif kind == "xq":
                    layernorm(X[:, item[1] * QT:(item[1] + 1) * QT, :])
                    flat = lambda x: x.rearrange("p q d -> p (q d)")
                    quantise(flat(XQ[:, :, :]), flat(X[:, item[1] * QT:(item[1] + 1) * QT, :]), P, QT * D)
                    v.engine_nop().then_inc(made, 1)
                elif kind == "hqT":
                    S["act"] += 1
                    dve.wait_ge(act_out, S["act"])
                    link(v.tensor_tensor(H[:, :, :], H[:, :, :], UP[:, :, :], ALU.mult))
                    flat = lambda x: x.rearrange("p q d -> p (q d)")
                    quantise(flat(H[:, :, :]), flat(H[:, :, :]), P, QT * FF)
                    v.engine_nop().then_inc(made, 1)
                elif kind == "x2T":
                    layernorm(X[:, item[1] * QT:(item[1] + 1) * QT, :])
                    v.engine_nop().then_inc(made, 1)
                elif kind == "x3T":
                    layernorm(R[:, :, :])
                    v.engine_nop().then_inc(made, 1)
                elif kind == "gwT":
                    gate_weights()
                    v.engine_nop().then_inc(made, 1)

            def gate_weights():
                bc = lambda x: x.broadcast_to([P, QT, NE])
                link(v.tensor_reduce(GM[:, :, :], GL[:, :, :], AX, ALU.max))
                link(v.tensor_tensor(GL[:, :, :], GL[:, :, :], bc(GM[:, :, :]), ALU.subtract))
                v.engine_nop().then_inc(act_in, 1)
                S["act"] = S["act"] + 1
                dve.wait_ge(act_out, S["act"])
                link(v.tensor_reduce(GS[:, :, :], GP[:, :, :], AX, ALU.add))
                link(v.reciprocal(GM[:, :, :], GS[:, :, :]))
                link(v.tensor_tensor(G2[:, :, :], GP[:, :, :], bc(GM[:, :, :]), ALU.mult))
                link(v.scalar_tensor_tensor(GW[:, :, :], G2[:, :, :], 0.1, G2[:, :, :], ALU.is_ge, ALU.mult))
                link(v.tensor_reduce(GS[:, :, :], GW[:, :, :], AX, ALU.add))
                link(v.scalar_tensor_tensor(GM[:, :, :], GS[:, :, :], 0.0, GS[:, :, :], ALU.is_equal, ALU.add))
                link(v.reciprocal(GS[:, :, :], GM[:, :, :]))
                link(v.tensor_tensor(GW[:, :, :], GW[:, :, :], bc(GS[:, :, :]), ALU.mult))

            def chunk_item(item, bank, free):
                kind = item[0]
                tiles = bank.rearrange("p (q d) -> p q d", d=D)
                if kind == "out0":
                    b = item[1]
                    o = bank.rearrange("p (q h l) -> p q h l", q=QT, h=2)
                    rec = OR[:, :, 0:2]
                    link(v.reciprocal(rec, o[:, :, :, LAT]))
                    v.tensor_tensor(ON[:, :, :].rearrange("p q (h l) -> p q h l", l=LAT)[:, :, 2 * b:2 * b + 2, :],
                                    o[:, :, :, 0:LAT], rec.unsqueeze(3).broadcast_to([P, QT, 2, LAT]), ALU.mult).then_inc(free, 1)
                elif kind == "out1":
                    g = item[1]
                    o = bank.rearrange("p (q h l) -> p q h l", q=QT, h=HG)
                    link(v.reciprocal(OR[:, :, :], o[:, :, :, HD1]))
                    v.tensor_tensor(ON[:, :, g * LAT:(g + 1) * LAT].rearrange("p q (h l) -> p q h l", l=HD1),
                                    o[:, :, :, 0:HD1], OR[:, :, :].unsqueeze(3).broadcast_to([P, QT, HG, HD1]),
                                    ALU.mult).then_inc(free, 1)
                elif kind in ("on0", "on1"):
                    v.tensor_copy(ONT[:, item[1] if kind == "on0" else 0, :], bank).then_inc(free, 1)
                elif kind == "y0":
                    link(v.tensor_tensor(R[:, :, :], tiles, X[:, item[1] * QT:(item[1] + 1) * QT, :], ALU.add))
                    v.engine_nop().then_inc(free, 1)
                elif kind == "y1":
                    c = item[1]
                    link(v.tensor_tensor(R[:, :, :], tiles, bo_b[:, :].unsqueeze(1).broadcast_to([P, QT, D]), ALU.add))
                    link(v.tensor_tensor(R[:, :, :], R[:, :, :], X[:, bass.ds(c * QT, QT), :], ALU.add))
                    v.engine_nop().then_inc(free, 1)
                elif kind == "xq":
                    v.tensor_copy(XQT[:, :], bank).then_inc(free, 1)
                elif kind == "gate":
                    v.tensor_copy(H[:, item[1], :], bank[:, 0:FF]).then_inc(free, 1)
                elif kind == "up":
                    link(v.tensor_copy(UP[:, item[1], :], bank[:, 0:FF]))
                    v.engine_nop().then_inc(free, 1)
                    if item[1] == QT - 1:
                        v.engine_nop().then_inc(act_in, 1)
                elif kind == "hqT":
                    q = item[1]
                    v.tensor_copy(HQT[:, q, 0:2, :], bank[:, 0:2 * P].rearrange("p (j d) -> p j d", d=D))
                    v.tensor_copy(HQT[0:FF - 2 * P, q, 2, :], bank[0:FF - 2 * P, 2 * P:3 * P]).then_inc(free, 1)
                elif kind == "down":
                    link(v.tensor_tensor(R[:, :, :], tiles, X[:, item[1] * QT:(item[1] + 1) * QT, :], ALU.add))
                    v.engine_nop().then_inc(free, 1)
                elif kind == "x2T":
                    v.tensor_copy(XT[:, item[1] * QC:(item[1] + 1) * QC], bank).then_inc(free, 1)
                elif kind == "x3T":
                    v.tensor_copy(X2T[:, :], bank).then_inc(free, 1)
                elif kind == "logits":
                    link(v.tensor_tensor(GL[:, :, :], bank[:, 0:QT * NE].rearrange("p (q e) -> p q e", e=NE),
                                         gb_b[:, :].unsqueeze(1).broadcast_to([P, QT, NE]), ALU.add))
                    v.engine_nop().then_inc(free, 1)
                elif kind == "gwT":
                    v.tensor_copy(GWT, bank[0:NE, :].rearrange("e (q p) -> e q p", p=P)).then_inc(free, 1)
                elif kind == "ebias":
                    link(v.tensor_tensor(ACC[:, :, :], tiles, R[:, :, :], ALU.add))
                    v.engine_nop().then_inc(free, 1)
                elif kind == "expert":
                    q, half = item[1:]
                    for e in range(4):
                        link(v.scalar_tensor_tensor(ACC[:, q, :], tiles[:, e, :], GW[:, q, 4 * half + e:4 * half + e + 1],
                                                    ACC[:, q, :], ALU.mult, ALU.add))
                    v.engine_nop().then_inc(free, 1)
                elif kind == "pad":
                    v.tensor_copy(OS[:, 0:P], bank[:, 0:P]).then_inc(free, 1)

            dve.wait_ge(ld["const"], 16)
            dve.wait_ge(consts_set, 1)
            v.memset(KO0[SHIFT:KR, :, :].bitcast(f32), 1.0)
            v.memset(KO1[SHIFT:KR, :, :].bitcast(f32), 1.0)
            v.tensor_copy(ident_b[:, :], ident)
            v.tensor_copy(mask_kq[:, :], const[:, P:2 * P])
            v.tensor_copy(mask_qk[:, :], const[:, 2 * P:3 * P])
            dve.wait_ge(ld["attn0"], 16 * 6)
            for g in range(G0):
                for r in range(3):
                    link(v.tensor_copy(WK3[:, g, r * LAT:(r + 1) * LAT], wkd[:, g * LAT:(g + 1) * LAT]))
            dve.wait_ge(ld["ffn0"], 16 * 5)
            for w in (wg, wu):
                two = w[:, 0:2, :].rearrange("p t d -> p (t d)")
                quantise(two, two, P, 2 * D)
                quantise(w[0:FF - 2 * P, 2, :], w[0:FF - 2 * P, 2, :], FF - 2 * P, D)
            quantise(wd[:, :], wd[:, :], P, FF)
            v.engine_nop().then_inc(weights_ready, 1)
            for item in prep + before(0, 0, 0, 0):
                side_item(item)
            for i, (c, g) in enumerate(iters0):
                for item in before(0, *iters0[i + 1], i + 1) if i + 1 < len(iters0) else []:
                    side_item(item)
                S["units"] += units0[i]
                S["pv"] = S["units"]
                for item in after0(c, g) + (chunk0(c) if g == G0 - 1 else []):
                    side_item(item)
            dve.wait_ge(ld["attn1"], N_ATTN1)
            dve.wait_ge(ld["moe"], 64)
            for item in start1 + [("pad",)] * PAD:
                side_item(item)

            def final(c):
                link(v.tensor_copy(R[:, :, :], ACC[:, :, :]))
                dve.wait_ge(stored, 16 * c + 16)
                layernorm(OUT)
                v.engine_nop().then_inc(tile_out, 1)

            def chunk(c, last):
                dve.sem_clear(chain)
                S.update(side=0, base=BASE1 + c * SIDE1, half=BASE1 // 2 + c * (SIDE1 // 2), links=0, rstd=2 * NC + 2 * c, act=NC + c, group=c * G1 + 1)
                steps, tail = plan1(c, last)
                for g, side in steps:
                    S["pv"] = NP_RING + UNITS0 + c * UNITS1 + g * NT * HG
                    for item in side:
                        side_item(item)
                S["pv"] = NP_RING + UNITS0 + c * UNITS1 + G1 * NT * HG
                for item in tail:
                    side_item(item)
                final(c)

            with dve.Fori(0, NC - 1) as c:
                chunk(c, False)
            chunk(NC - 1, True)


_INS = ['L0_attn_x', 'L0_attn_wq', 'L0_attn_wk_down', 'L0_attn_wv_down', 'L0_attn_wk_up', 'L0_attn_wv_up',
        'L0_attn_wo', 'L0_ffn_w_gate', 'L0_ffn_w_up', 'L0_ffn_w_down', 'L1_attn_Wq', 'L1_attn_bq', 'L1_attn_Wk',
        'L1_attn_bk', 'L1_attn_Wv', 'L1_attn_bv', 'L1_attn_Wo', 'L1_attn_bo', 'L1_ffn_gate_w', 'L1_ffn_gate_b',
        'L1_ffn_expert_w', 'L1_ffn_expert_b']


def kernel(**inputs):
    import concourse.bacc as bacc
    from concourse.bass_utils import run_bass_kernel_spmd

    nc = bacc.Bacc("TRN2", target_bir_lowering=False, num_devices=1)
    arrays = {name: np.ascontiguousarray(inputs[name]) for name in _INS}
    arrays["consts"] = constants()
    A = {name: nc.dram_tensor("in_" + name, a.shape, mybir.dt.from_np(a.dtype), kind="ExternalInput").ap()
         for name, a in arrays.items()}
    A["out"] = nc.dram_tensor("result", (1, T, D), mybir.dt.float32, kind="ExternalOutput").ap()
    build(nc, A)
    r = run_bass_kernel_spmd(nc, [{"in_" + name: a for name, a in arrays.items()}], core_ids=[0])
    return r.results[0]["result"]
```
